# Optimizing a Trainium2 kernel written in Bass

```python
import numpy as np
import jax
import jax.numpy as jnp

def _softmax(x, axis=-1):
    return jax.nn.softmax(x, axis=axis)

def _gelu(x):
    return jax.nn.gelu(x, approximate=True)

def _silu(x):
    return jax.nn.silu(x)

def _sigmoid(x):
    return jax.nn.sigmoid(x)

def _layernorm(x, axis=-1, eps=1e-05):
    m = jnp.mean(x, axis=axis, keepdims=True)
    v = jnp.var(x, axis=axis, keepdims=True)
    return (x - m) / jnp.sqrt(v + eps)

def _scatter_add(tgt, idx, src, axis=0):
    return tgt.at[idx].add(src)

def _segment_sum(src, seg, n):
    return jax.ops.segment_sum(src, seg, n)
kernel_name = 'mk_cond_resid_d2_seqx_r8_de8ce0'

def setup_inputs(seed: int=0):
    np.random.seed(seed)
    _w = jnp.asarray

    def _rec_inputs():
        import jax
        import jax.numpy as jnp
        _rk = jax.random.key(seed)
        x = -0.0005207 + 1.001 * jax.random.normal(jax.random.fold_in(_rk, 1), (16, 128, 128), jnp.float32)
        _lenS = 128 - jax.random.randint(jax.random.fold_in(_rk, 7), (16,), 0, max(1, 128 // 4) + 1, jnp.int32)
        _lenS2 = 128 - jax.random.randint(jax.random.fold_in(_rk, 8), (16,), 0, max(1, 128 // 4) + 1, jnp.int32)
        fside_Bx8_0 = jax.random.uniform(jax.random.fold_in(_rk, 11), (16, 8), jnp.float32, 0.0, 0.556406)
        condB_sharedgateprob = jax.random.uniform(jax.random.fold_in(_rk, 12), (16,), jnp.float32, 0.0, 0.794948)
        itok_B_1_98 = jax.random.randint(jax.random.fold_in(_rk, 13), (16,), 1, 99, jnp.int32)
        return (x, fside_Bx8_0, condB_sharedgateprob, itok_B_1_98)
    x, fside_Bx8_0, condB_sharedgateprob, itok_B_1_98 = _rec_inputs()

    def _L0_cond_setup():
        import jax, jax.numpy as jnp
        import numpy as np
        E, B, S, D, F = (8, 2, 128, 128, 512)
        key = jax.random.key(seed)
        ks = jax.random.split(key, 9)
        sc_d = 1.0 / np.sqrt(D)
        sc_f = 1.0 / np.sqrt(F)
        hidden_states = jax.random.normal(ks[0], (B, S, D), dtype=jnp.float32)
        gating_probs = jax.nn.softmax(jax.random.normal(ks[1], (B, E), dtype=jnp.float32), axis=-1)
        shared_gate_prob = jax.nn.sigmoid(jax.random.normal(ks[2], (B, 1), dtype=jnp.float32))
        Wg = jax.random.normal(ks[3], (E, D, F), dtype=jnp.float32) * sc_d
        Wu = jax.random.normal(ks[4], (E, D, F), dtype=jnp.float32) * sc_d
        Wd = jax.random.normal(ks[5], (E, F, D), dtype=jnp.float32) * sc_f
        Sg = jax.random.normal(ks[6], (D, F), dtype=jnp.float32) * sc_d
        Su = jax.random.normal(ks[7], (D, F), dtype=jnp.float32) * sc_d
        Sd = jax.random.normal(ks[8], (F, D), dtype=jnp.float32) * sc_f
        return {'hidden_states': hidden_states, 'gating_probs': gating_probs, 'shared_gate_prob': shared_gate_prob, 'Wg': Wg, 'Wu': Wu, 'Wd': Wd, 'Sg': Sg, 'Su': Su, 'Sd': Sd}
    _L0_cond_all = _L0_cond_setup()
    _L0_cond_in = {k: v for k, v in _L0_cond_all.items() if k in ('Wg', 'Wu', 'Wd', 'Sg', 'Su', 'Sd')}
    del _L0_cond_all

    def _L1_cond_setup():
        import jax, jax.numpy as jnp
        import numpy as np
        B = 128
        D = 128
        K = 100
        key = jax.random.key(seed)
        kx, kt, ks = jax.random.split(key, 3)
        x = jax.random.normal(kx, (B, D, D), dtype=jnp.float32)
        T = jax.random.normal(kt, (K, D, D), dtype=jnp.float32)
        fwd_steps = jax.random.randint(ks, (B,), 1, K + 1, dtype=jnp.int64)
        return {'x': x, 'fwd_steps': fwd_steps, 'T': T}
    _L1_cond_all = _L1_cond_setup()
    _L1_cond_in = {k: v for k, v in _L1_cond_all.items() if k in ('T',)}
    del _L1_cond_all
    return {'x': x, 'fside_Bx8_0': fside_Bx8_0, 'condB_sharedgateprob': condB_sharedgateprob, 'itok_B_1_98': itok_B_1_98, 'L0_cond_Wg': _L0_cond_in['Wg'], 'L0_cond_Wu': _L0_cond_in['Wu'], 'L0_cond_Wd': _L0_cond_in['Wd'], 'L0_cond_Sg': _L0_cond_in['Sg'], 'L0_cond_Su': _L0_cond_in['Su'], 'L0_cond_Sd': _L0_cond_in['Sd'], 'L1_cond_T': _L1_cond_in['T']}

def reference(x, fside_Bx8_0, condB_sharedgateprob, itok_B_1_98, L0_cond_Wg, L0_cond_Wu, L0_cond_Wd, L0_cond_Sg, L0_cond_Su, L0_cond_Sd, L1_cond_T):
    import jax
    import jax.numpy as jnp

    def _L0_cond_ref(hidden_states, gating_probs, shared_gate_prob, Wg, Wu, Wd, Sg, Su, Sd):
        import jax, jax.numpy as jnp
        import numpy as np
        E, B, S, D, F = (8, 2, 128, 128, 512)
        h = hidden_states
        g = jnp.einsum('bsd,edf->ebsf', h, Wg)
        u = jnp.einsum('bsd,edf->ebsf', h, Wu)
        expert_outs = jnp.einsum('ebsf,efd->ebsd', jax.nn.silu(g) * u, Wd)
        expert_output = jnp.einsum('be,ebsd->bsd', gating_probs, expert_outs)
        shared = jnp.einsum('bsf,fd->bsd', jax.nn.silu(h @ Sg) * (h @ Su), Sd)
        sg = shared_gate_prob[:, :, None]
        return (1.0 - sg) * expert_output + sg * shared

    def _L1_cond_ref(x, fwd_steps, T):
        import jax, jax.numpy as jnp
        import numpy as np
        B = 128
        D = 128
        K = 100
        Tb = T[fwd_steps - 1]
        return jnp.einsum('bij,bjk->bik', Tb, x)
    x = x + _L0_cond_ref(x, fside_Bx8_0, condB_sharedgateprob[:, None], L0_cond_Wg, L0_cond_Wu, L0_cond_Wd, L0_cond_Sg, L0_cond_Su, L0_cond_Sd)
    x = x + _L1_cond_ref(x, itok_B_1_98, L1_cond_T)
    return x

_drawn_inputs = setup_inputs


def setup_inputs(seed=0):
    import zlib

    import numpy as np

    out = dict(_drawn_inputs(seed))
    spreads = {}
    factors = {}
    for name, (base, spread) in spreads.items():
        noise = np.random.default_rng([zlib.crc32(name.encode()), seed]).standard_normal(out[name].shape)
        drawn = base * np.exp(spread * noise) if base else spread * noise
        out[name] = jnp.asarray(drawn.astype(out[name].dtype))
    for name, factor in factors.items():
        out[name] = (out[name] * factor).astype(out[name].dtype)
    return out
```

```python
from contextlib import ExitStack

import concourse.bass as bass
from concourse import mybir

P = 128
F32 = mybir.dt.float32
F32R = mybir.dt.float32r
ALU = mybir.AluOpType
ACT = mybir.ActivationFunctionType


def moe_then_step_kernel(
    nc: bass.Bass,
    x: bass.AP,
    route: bass.AP,
    share: bass.AP,
    step: bass.AP,
    Wg: bass.AP,
    Wu: bass.AP,
    Wd: bass.AP,
    Sg: bass.AP,
    Su: bass.AP,
    Sd: bass.AP,
    T: bass.AP,
    out: bass.AP,
):
    B, S, D = x.shape
    E, _, F = Wg.shape
    K = T.shape[0]
    assert S == P and D == P
    NC = F // P
    BT = 4
    NT = B // BT
    W = BT * S
    U = NT * NC
    N_ROUTED = E * U
    N = N_ROUTED + U
    HR = 4
    LAG = 2
    assert NC == 4 and NT == 4 and E % 2 == 0

    with ExitStack() as ctx:
        def sb(name, shape, dt=F32):
            return ctx.enter_context(nc.sbuf_tensor(name, shape, dt))

        def sem(name):
            return ctx.enter_context(nc.semaphore(name))

        x_nat = sb("x_nat", [P, B, D])
        x_hi = sb("x_hi", [P, NT, W], F32R)
        x_lo = sb("x_lo", [P, NT, W], F32R)
        w_raw = sb("w_raw", [P, 2, NC, 3, P])
        w_hi = sb("w_hi", [P, 2, NC, 3, P], F32R)
        w_lo = sb("w_lo", [P, 2, NC, 3, P], F32R)
        silu_g = sb("silu_g", [P, 2, W])
        h_hi = sb("h_hi", [P, HR, W], F32R)
        h_lo = sb("h_lo", [P, HR, W], F32R)
        scaled = sb("scaled", [P, 2, W])
        acc = sb("acc", [P, NT, W])
        yT = sb("yT", [P, NT, W])
        y = sb("y", [P, B, D])
        res = sb("res", [P, B, D])
        T_nat = sb("T_nat", [P, B, P])
        T_plus = sb("T_plus", [P, B, P])
        ident = sb("ident", [P, P])
        route_b = sb("route_b", [P, B, E])
        share_b = sb("share_b", [P, B])
        rest_b = sb("rest_b", [P, B])
        coef = sb("coef", [P, (E + 1) * B])

        g_bank = [ctx.enter_context(nc.psum_tensor(f"g_bank{i}", [P, W], F32)) for i in range(2)]
        u_bank = [ctx.enter_context(nc.psum_tensor(f"u_bank{i}", [P, W], F32)) for i in range(HR)]
        o_bank = [ctx.enter_context(nc.psum_tensor(f"o_bank{i}", [P, W], F32)) for i in range(2)]

        x_in = [sem(f"x_in{t}") for t in range(NT)]
        w0_in = [sem(f"w0_in{c}") for c in range(NC)]
        w_in = [sem(f"w_in{s}") for s in range(2)]
        c_in = sem("c_in")
        T_in = sem("T_in")
        ident_done = sem("ident_done")
        coef_step = sem("coef_step")
        x_turned = sem("x_turned")
        x_rounded = sem("x_rounded")
        w_hi_done = sem("w_hi_done")
        w_ready = sem("w_ready")
        g_done = sem("g_done")
        g_read = sem("g_read")
        u_done = sem("u_done")
        h_done = sem("h_done")
        h_rounded = sem("h_rounded")
        split_done = sem("split_done")
        o_done = sem("o_done")
        scaled_done = sem("scaled_done")
        acc_done = sem("acc_done")
        T_done = sem("T_done")
        yT_done = sem("yT_done")
        y_turned = sem("y_turned")
        y_done = sem("y_done")
        r_done = sem("r_done")
        res_done = sem("res_done")
        stored = sem("stored")

        parts = [(t * BT, BT) for t in range(NT - 1)] + [((NT - 1) * BT + b, 1) for b in range(BT)]
        last_part = len(parts) - 1
        parts_of = [[i for i, (b, _) in enumerate(parts) if b // BT == t] for t in range(NT)]

        def part_bank(i):
            b, nb = parts[i]
            return o_bank[(b // BT) % 2] if nb == BT else u_bank[b % BT]

        FIRST_TURN = N_ROUTED + LAG + 1

        def turned_before(n):
            return min(max(n - FIRST_TURN + 1, 0), NT) if isinstance(n, int) else 0

        def turn_fill(t):
            return FIRST_TURN + 2 * t

        STEP_AT = [N_ROUTED + NC * t + 9 for t in range(NT - 1)]

        block = ctx.enter_context(nc.Block())

        @block.sync
        def _(sp):
            def load_tile(t):
                sp.dma_start(x_nat[:, t * BT:(t + 1) * BT, :],
                             x[t * BT:(t + 1) * BT, :, :].rearrange("b s d -> s b d")).then_inc(x_in[t], 16)

            def load_expert(slot, gate, up, down):
                sp.dma_start(w_raw[:, slot, :, 0, :], gate.rearrange("p (c f) -> p c f", c=NC)).then_inc(w_in[slot], 16)
                sp.dma_start(w_raw[:, slot, :, 1, :], up.rearrange("p (c f) -> p c f", c=NC)).then_inc(w_in[slot], 16)
                sp.dma_start(w_raw[:, slot, :, 2, :], down.rearrange("(c p) d -> p c d", p=P)).then_inc(w_in[slot], 16)

            def of_pair(w, pair, slot):
                pairs = w.rearrange("(i s) p f -> i s p f", s=2)
                return pairs[bass.ds(pair, 1), slot, :, :].rearrange("i p f -> (i p) f")

            load_tile(0)
            for c in range(NC):
                f = slice(c * P, (c + 1) * P)
                sp.dma_start(w_raw[:, 0, c, 0, :], Wg[0, :, f]).then_inc(w0_in[c], 16)
                sp.dma_start(w_raw[:, 0, c, 1, :], Wu[0, :, f]).then_inc(w0_in[c], 16)
                sp.dma_start(w_raw[:, 0, c, 2, :], Wd[0, f, :]).then_inc(w0_in[c], 16)
                if c < NT - 1:
                    load_tile(c + 1)
            load_expert(1, Wg[1, :, :], Wu[1, :, :], Wd[1, :, :])
            with sp.Fori(0, B) as b:
                which = sp.value_load(step[bass.ds(b, 1)].rearrange("(a n) -> a n", a=1), min_val=1, max_val=K)
                sp.dma_start(T_nat[:, bass.ds(b, 1), :],
                             T[bass.ds(which - 1, 1), :, :].rearrange("a i j -> i a j")).then_inc(T_in, 16)
            with sp.Fori(1, E // 2) as pair:
                for slot in range(2):
                    sp.wait_ge(w_ready, 2 * NC * pair + NC * (slot - 1))
                    load_expert(slot, of_pair(Wg, pair, slot), of_pair(Wu, pair, slot), of_pair(Wd, pair, slot))
            sp.wait_ge(w_ready, NC * (E - 1))
            load_expert(0, Sg[:, :], Su[:, :], Sd[:, :])

            for i, (b, nb) in enumerate(parts):
                sp.wait_ge(res_done, i + 1)
                sp.dma_start(out[b:b + nb, :, :].rearrange("b s d -> s b d"), res[:, b:b + nb, :]).then_inc(stored, 16)
            sp.wait_ge(stored, 16 * len(parts))

        @block.gpsimd
        def _(pool):
            pool.dma_start(route_b[:, :, :], route.rearrange("(a b) e -> a b e", a=1).to_broadcast([P, B, E])).then_inc(c_in, 16)
            pool.dma_start(share_b[:, :], share.rearrange("(a b) -> a b", a=1).to_broadcast([P, B])).then_inc(c_in, 16)
            nc.gpsimd.memset(ident[:, :], 0.0).then_inc(ident_done, 1)
            pool.wait_ge(ident_done, 1)
            nc.gpsimd.affine_select(out=ident[:, :], in_=ident[:, :], compare_op=ALU.not_equal, fill=1.0, base=0,
                                    pattern=[[-1, P]], channel_multiplier=1).then_inc(ident_done, 1)

            def split_chunk(slot, c, count):
                nc.gpsimd.tensor_copy(w_hi[:, slot, c, :, :], w_raw[:, slot, c, :, :]).then_inc(w_hi_done, 1)
                pool.wait_ge(w_hi_done, count + 1)
                nc.gpsimd.tensor_tensor(w_lo[:, slot, c, :, :], w_raw[:, slot, c, :, :],
                                        w_hi[:, slot, c, :, :].bitcast(F32), ALU.subtract).then_inc(w_ready, 1)

            for c in range(NC):
                pool.wait_ge(w0_in[c], 48)
                split_chunk(0, c, c)
            nc.gpsimd.memset(acc[:, 0:NT // 2, :], 0.0).then_inc(acc_done, 1)
            nc.gpsimd.memset(acc[:, NT // 2:NT, :], 0.0).then_inc(acc_done, 1)

            pool.wait_ge(c_in, 32)
            nc.gpsimd.tensor_scalar(rest_b[:, :], share_b[:, :], -1.0, 1.0, ALU.mult, ALU.add).then_inc(coef_step, 1)
            nc.gpsimd.tensor_copy(coef[:, E * B:(E + 1) * B], share_b[:, :]).then_inc(coef_step, 1)
            pool.wait_ge(coef_step, 2)
            nc.gpsimd.tensor_tensor(coef[:, 0:E * B].rearrange("p (e b) -> p b e", b=B), route_b[:, :, :],
                                    rest_b[:, :].unsqueeze(2).to_broadcast([P, B, E]), ALU.mult).then_inc(coef_step, 1)

            with pool.Fori(0, E, 2) as e:
                for par in range(2):
                    slot = (par + 1) % 2
                    for t in range(NT):
                        group = NT * (e + par) + t
                        if t == 0:
                            pool.wait_ge(w_in[slot], 24 * e + 48)
                        pool.wait_ge(acc_done, group + 2)
                        pool.wait_ge(scaled_done, group + 1)
                        nc.gpsimd.tensor_tensor(acc[:, t, :], acc[:, t, :], scaled[:, t % 2, :], ALU.add).then_inc(acc_done, 1)
                        if t < 2:
                            for c in (2 * t, 2 * t + 1):
                                split_chunk(slot, c, NC * (e + par + 1) + c)

            for t in range(NT):
                pool.wait_ge(g_read, turn_fill(t) + 1)
                turned = T_plus[:, t * BT:(t + 1) * BT, :]
                nc.gpsimd.tensor_tensor(turned, turned, ident[:, :].unsqueeze(1).to_broadcast([P, BT, P]),
                                        ALU.add).then_inc(T_done, 1)

        @block.scalar
        def _(act):
            def silu(n, k, turned):
                act.wait_ge(g_done, n + turned + 1)
                nc.scalar.activation(silu_g[:, k % 2, :], g_bank[(k + turned) % 2][:, :], ACT.Silu).then_inc(g_read, 1)

            def round_h(n, k):
                act.wait_ge(h_done, n + 1)
                nc.scalar.activation(h_hi[:, k % HR, :], u_bank[k % HR][:, :], ACT.Copy).then_inc(h_rounded, 1)

            def copy_result(i):
                b, nb = parts[i]
                act.wait_ge(r_done, i + 1)
                nc.scalar.activation(res[:, b:b + nb, :], part_bank(i)[:, 0:nb * D].rearrange("p (b d) -> p b d", b=nb),
                                     ACT.Copy).then_inc(res_done, 1)

            for t in range(NT):
                act.wait_ge(x_turned, t + 1)
                nc.scalar.activation(x_hi[:, t, :], u_bank[t][:, :], ACT.Copy).then_inc(x_rounded, 1)
            silu(0, 0, 0)
            with act.Fori(0, N_ROUTED, U) as n0:
                for k in range(1, U + 1):
                    silu(n0 + k, k, 0)
                    round_h(n0 + k - 1, k - 1)
            for n in range(N_ROUTED + 1, N + LAG):
                if n - FIRST_TURN in range(NT):
                    t = n - FIRST_TURN
                    act.wait_ge(g_done, turn_fill(t) + 1)
                    nc.scalar.activation(T_plus[:, t * BT:(t + 1) * BT, :],
                                         g_bank[turn_fill(t) % 2][:, :].rearrange("p (b i) -> p b i", b=BT),
                                         ACT.Copy).then_inc(g_read, 1)
                if n < N:
                    silu(n, n, turned_before(n))
                if n - 1 < N:
                    round_h(n - 1, n - 1)
                for t in range(NT - 1):
                    if n == STEP_AT[t]:
                        copy_result(t)
            for i in range(NT - 1, len(parts)):
                copy_result(i)

        @block.vector
        def _(dve):
            def make_h(n, k):
                dve.wait_ge(g_read, n + turned_before(n) + 1)
                dve.wait_ge(u_done, n + 1)
                nc.vector.tensor_tensor(u_bank[k % HR][:, :], u_bank[k % HR][:, :], silu_g[:, k % 2, :],
                                        ALU.mult).then_inc(h_done, 1)

            def split_h(n, k):
                dve.wait_ge(h_rounded, n + 1)
                nc.vector.tensor_tensor(h_lo[:, k % HR, :], u_bank[k % HR][:, :], h_hi[:, k % HR, :].bitcast(F32),
                                        ALU.subtract).then_inc(split_done, 1)

            def scale_group(m0, t):
                dve.wait_ge(o_done, m0 + t + 1)
                dve.wait_ge(acc_done, m0 + t + 1)
                nc.vector.tensor_tensor(scaled[:, t % 2, :].rearrange("p (b s) -> p b s", b=BT),
                                        o_bank[t % 2][:, :].rearrange("p (b s) -> p b s", b=BT),
                                        coef[:, bass.ds(m0 * BT + t * BT, BT)].unsqueeze(2).to_broadcast([P, BT, S]),
                                        ALU.mult).then_inc(scaled_done, 1)

            def add_shared(b):
                t, j = divmod(b, BT)
                s = slice(j * S, (j + 1) * S)
                nc.vector.scalar_tensor_tensor(out=yT[:, t, s], in0=o_bank[t % 2][:, s], scalar=coef[:, E * B + b:E * B + b + 1],
                                               in1=acc[:, t, s], op0=ALU.mult, op1=ALU.add).then_inc(yT_done, 1)

            def add_x(i):
                b, nb = parts[i]
                dve.wait_ge(y_turned, i + 1)
                nc.vector.tensor_tensor(y[:, b:b + nb, :], part_bank(i)[:, 0:nb * D].rearrange("p (b d) -> p b d", b=nb),
                                        x_nat[:, b:b + nb, :], ALU.add).then_inc(y_done, 1)

            for t in range(NT):
                dve.wait_ge(x_rounded, t + 1)
                nc.vector.tensor_tensor(x_lo[:, t, :], u_bank[t][:, :], x_hi[:, t, :].bitcast(F32),
                                        ALU.subtract).then_inc(split_done, 1)
            make_h(0, 0)
            make_h(1, 1)
            split_h(0, 0)
            make_h(2, 2)
            split_h(1, 1)
            dve.wait_ge(coef_step, 3)
            with dve.Fori(0, E * NT, NT) as m0:
                for k in range(3, U + 3):
                    if k in range(NC + LAG, U + 3, NC):
                        scale_group(m0, (k - NC - LAG) // NC)
                    make_h(m0 * NC + k, k)
                    split_h(m0 * NC + k - 1, k - 1)
            for n in range(N_ROUTED + 3, N + 1):
                for t in range(NT - 1):
                    if n == STEP_AT[t] - 1:
                        add_x(t)
                    if n == STEP_AT[t] - 3:
                        dve.wait_ge(o_done, E * NT + t + 1)
                        dve.wait_ge(acc_done, 2 + E * NT)
                        for b in range(t * BT, (t + 1) * BT):
                            add_shared(b)
                if n < N:
                    make_h(n, n)
                split_h(n - 1, n - 1)
            for t in range(NT - 1):
                if STEP_AT[t] - 1 > N:
                    add_x(t)
            dve.wait_ge(o_done, E * NT + NT)
            for j in range(BT):
                add_shared((NT - 1) * BT + j)
                if j:
                    add_x(NT - 2 + j)
            add_x(len(parts) - 1)

        @block.tensor
        def _(pe):
            def product(bank, w, x_h, x_l, start, stop):
                nc.tensor.matmul(bank, w_hi[:, w[0], w[1], w[2], :], x_h, start=start, stop=False)
                nc.tensor.matmul(bank, w_hi[:, w[0], w[1], w[2], :], x_l, start=False, stop=False)
                return nc.tensor.matmul(bank, w_lo[:, w[0], w[1], w[2], :], x_h, start=False, stop=stop)

            def turn_x(t):
                pe.wait_ge(x_in[t], 16)
                for j in range(BT):
                    last = nc.tensor.transpose(u_bank[t][:, j * S:(j + 1) * S], x_nat[:, t * BT + j, :], ident[:, :])
                last.then_inc(x_turned, 1)

            def project_g(n, k, e, turned):
                t, c = k % U // NC, k % NC
                if not (isinstance(n, int) and n < 2):
                    pe.wait_ge(g_read, n + turned - 1)
                if t == 0:
                    pe.wait_ge(w_ready, e * NC + c + 1)
                product(g_bank[(k + turned) % 2][:, :], (k // U % 2, c, 0), x_hi[:, t, :], x_lo[:, t, :],
                        True, True).then_inc(g_done, 1)

            def project_u(n, k):
                t, c = k % U // NC, k % NC
                pe.wait_ge(split_done, n + 1)
                product(u_bank[k % HR][:, :], (k // U % 2, c, 1), x_hi[:, t, :], x_lo[:, t, :],
                        True, True).then_inc(u_done, 1)

            def project_down(n, k):
                t, c = k % U // NC, k % NC
                pe.wait_ge(split_done, NT + n + 1)
                last = product(o_bank[t % 2][:, :], (k // U % 2, c, 2), h_hi[:, k % HR, :], h_lo[:, k % HR, :],
                               c == 0, c == NC - 1)
                if c == NC - 1:
                    last.then_inc(o_done, 1)

            def turn_y(i):
                b, nb = parts[i]
                pe.wait_ge(yT_done, b + nb)
                for j in range(nb):
                    t, s = (b + j) // BT, ((b + j) % BT) * S
                    last = nc.tensor.transpose(part_bank(i)[:, j * D:(j + 1) * D], yT[:, t, s:s + S], ident[:, :])
                last.then_inc(y_turned, 1)

            def step_y(i):
                b, nb = parts[i]
                pe.wait_ge(y_done, i + 1)
                for j in range(nb):
                    last = nc.tensor.matmul(part_bank(i)[:, j * D:(j + 1) * D], T_plus[:, b + j, :], y[:, b + j, :],
                                            start=True, stop=True)
                last.then_inc(r_done, 1)

            pe.wait_ge(ident_done, 2)
            turn_x(0)
            pe.wait_ge(split_done, 1)
            project_g(0, 0, 0, 0)
            turn_x(1)
            project_u(0, 0)
            turn_x(2)
            project_g(1, 1, 0, 0)
            turn_x(3)
            project_u(1, 1)
            with pe.Fori(0, N_ROUTED // U, 2) as e:
                for k in range(LAG, 2 * U + LAG):
                    project_g(e * U + k, k, e + k // U, 0)
                    project_u(e * U + k, k)
                    project_down(e * U + k - LAG, k - LAG)
            pe.wait_ge(T_in, 16 * B)
            for n in range(N_ROUTED + LAG, N + LAG):
                if n - FIRST_TURN in range(NT):
                    t = n - FIRST_TURN
                    pe.wait_ge(g_read, turn_fill(t) - 1)
                    for j in range(BT):
                        last = nc.tensor.transpose(g_bank[turn_fill(t) % 2][:, j * P:(j + 1) * P], T_nat[:, t * BT + j, :],
                                                   ident[:, :])
                    last.then_inc(g_done, 1)
                for t in range(NT - 1):
                    if n == STEP_AT[t] - 2:
                        turn_y(t)
                    if n == STEP_AT[t]:
                        if t == 0:
                            pe.wait_ge(T_done, NT)
                        step_y(t)
                if n < N:
                    project_g(n, n, E, turned_before(n))
                    project_u(n, n)
                m = (n - LAG - N_ROUTED) // NC
                if (n - LAG) % NC == 0 and m >= 2:
                    pe.wait_ge(res_done, m - 1)
                project_down(n - LAG, n - LAG)
            for j in range(BT):
                turn_y(NT - 1 + j)
                if j:
                    step_y(NT - 2 + j)
            step_y(len(parts) - 1)


_INS = ["x", "fside_Bx8_0", "condB_sharedgateprob", "itok_B_1_98", "L0_cond_Wg", "L0_cond_Wu", "L0_cond_Wd",
        "L0_cond_Sg", "L0_cond_Su", "L0_cond_Sd", "L1_cond_T"]


def kernel(**inputs):
    import numpy as _np
    import concourse.bacc as _bacc
    from concourse import mybir as _mybir
    from concourse.bass_utils import run_bass_kernel_spmd as _run

    nc = _bacc.Bacc("TRN2", target_bir_lowering=False, num_devices=1)
    arrays, args = {}, []
    for name in _INS:
        a = _np.ascontiguousarray(inputs[name])
        arrays[f"in_{name}"] = a
        args.append(nc.dram_tensor(f"in_{name}", a.shape, _mybir.dt.from_np(a.dtype), kind="ExternalInput").ap())
    args.append(nc.dram_tensor("out_y", inputs["x"].shape, _mybir.dt.float32, kind="ExternalOutput").ap())
    moe_then_step_kernel(nc, *args)
    r = _run(nc, [arrays], core_ids=[0])
    return r.results[0]["out_y"]
```

```python
from contextlib import ExitStack

import concourse.bass as bass
from concourse import mybir

P = 128
F32 = mybir.dt.float32
F32R = mybir.dt.float32r
ALU = mybir.AluOpType
ACT = mybir.ActivationFunctionType


def moe_then_step_kernel(
    nc: bass.Bass,
    x: bass.AP,
    route: bass.AP,
    share: bass.AP,
    step: bass.AP,
    Wg: bass.AP,
    Wu: bass.AP,
    Wd: bass.AP,
    Sg: bass.AP,
    Su: bass.AP,
    Sd: bass.AP,
    T: bass.AP,
    out: bass.AP,
):
    B, S, D = x.shape
    E, _, F = Wg.shape
    K = T.shape[0]
    assert S == P and D == P
    NC = F // P
    BT = 4
    NT = B // BT
    W = BT * S
    U = NT * NC
    N_ROUTED = E * U
    N = N_ROUTED + U
    HR = 4
    LAG = 2
    EARLY = 3
    X_ORDER = (0, 1, 3, 2)
    assert NC == 4 and NT == 4 and E % 2 == 0

    with ExitStack() as ctx:
        def sb(name, shape, dt=F32):
            return ctx.enter_context(nc.sbuf_tensor(name, shape, dt))

        def sem(name):
            return ctx.enter_context(nc.semaphore(name))

        x_nat = sb("x_nat", [P, B, D])
        warm = sb("warm", [P, 1])
        x_hi = sb("x_hi", [P, NT, W], F32R)
        x_lo = sb("x_lo", [P, NT, W], F32R)
        w_raw = sb("w_raw", [P, 2, NC, 3, P])
        w_hi = sb("w_hi", [P, 2, NC, 3, P], F32R)
        w_lo = sb("w_lo", [P, 2, NC, 3, P], F32R)
        silu_g = sb("silu_g", [P, 2, W])
        h_hi = sb("h_hi", [P, HR, W], F32R)
        h_lo = sb("h_lo", [P, HR, W], F32R)
        scaled = sb("scaled", [P, 2, W])
        acc = sb("acc", [P, NT, W])
        yT = sb("yT", [P, NT, W])
        y = sb("y", [P, B, D])
        res = sb("res", [P, B, D])
        T_nat = sb("T_nat", [P, B, P])
        T_plus = sb("T_plus", [P, B, P])
        ident = sb("ident", [P, P])
        route_b = sb("route_b", [P, B, E])
        share_b = sb("share_b", [P, B])
        rest_b = sb("rest_b", [P, B])
        coef = sb("coef", [P, (E + 1) * B])

        g_bank = [ctx.enter_context(nc.psum_tensor(f"g_bank{i}", [P, W], F32)) for i in range(2)]
        u_bank = [ctx.enter_context(nc.psum_tensor(f"u_bank{i}", [P, W], F32)) for i in range(HR)]
        o_bank = [ctx.enter_context(nc.psum_tensor(f"o_bank{i}", [P, W], F32)) for i in range(2)]

        x_in = [sem(f"x_in{t}") for t in range(NT)]
        wg0_in = sem("wg0_in")
        wu0_in = sem("wu0_in")
        w0_in = sem("w0_in")
        wd0_in = sem("wd0_in")
        w_in = [sem(f"w_in{s}") for s in range(2)]
        c_in = sem("c_in")
        T_in = sem("T_in")
        warm_done = sem("warm_done")
        ident_done = sem("ident_done")
        coef_step = sem("coef_step")
        x_turned = sem("x_turned")
        x_rounded = sem("x_rounded")
        x_kept = sem("x_kept")
        x_kept_late = sem("x_kept_late")
        w0_rounded = sem("w0_rounded")
        w_rounded = sem("w_rounded")
        w_ready = sem("w_ready")
        g_done = sem("g_done")
        g_read = sem("g_read")
        u_done = sem("u_done")
        h_done = sem("h_done")
        h_rounded = sem("h_rounded")
        split_done = sem("split_done")
        o_done = sem("o_done")
        scaled_done = sem("scaled_done")
        acc_done = sem("acc_done")
        T_done = sem("T_done")
        yT_done = sem("yT_done")
        y_turned = sem("y_turned")
        y_done = sem("y_done")
        r_done = sem("r_done")
        res_done = sem("res_done")
        stored = sem("stored")

        x_bank = [u_bank[3], o_bank[0], o_bank[1], u_bank[3]]

        parts = [(t * BT, BT) for t in range(NT - 1)] + [((NT - 1) * BT + b, 1) for b in range(BT)]
        last_part = len(parts) - 1
        parts_of = [[i for i, (b, _) in enumerate(parts) if b // BT == t] for t in range(NT)]

        def part_bank(i):
            b, nb = parts[i]
            return o_bank[(b // BT) % 2] if nb == BT else u_bank[b % BT]

        FIRST_TURN = N_ROUTED + LAG + 1

        def turned_before(n):
            return min(max(n - FIRST_TURN + 1, 0), NT) if isinstance(n, int) else 0

        def turn_fill(t):
            return FIRST_TURN + 2 * t

        SCALE = [N_ROUTED + NC * t + NC + LAG for t in range(NT - 1)]
        TURN = [n + 1 for n in SCALE]
        COPY = [n + 2 for n in SCALE]
        STEP = [n + 3 for n in SCALE]

        block = ctx.enter_context(nc.Block())

        @block.sync
        def _(sp):
            def load_tile(t):
                sp.dma_start(x_nat[:, t * BT:(t + 1) * BT, :],
                             x[t * BT:(t + 1) * BT, :, :].rearrange("b s d -> s b d")).then_inc(x_in[t], 16)

            def load_expert(slot, gate, up, down):
                sp.dma_start(w_raw[:, slot, :, 0, :], gate.rearrange("p (c f) -> p c f", c=NC)).then_inc(w_in[slot], 16)
                sp.dma_start(w_raw[:, slot, :, 1, :], up.rearrange("p (c f) -> p c f", c=NC)).then_inc(w_in[slot], 16)
                sp.dma_start(w_raw[:, slot, :, 2, :], down.rearrange("(c p) d -> p c d", p=P)).then_inc(w_in[slot], 16)

            def of_pair(w, pair, slot):
                pairs = w.rearrange("(i s) p f -> i s p f", s=2)
                return pairs[bass.ds(pair, 1), slot, :, :].rearrange("i p f -> (i p) f")

            rest = slice(P, F)
            load_tile(0)
            sp.dma_start(w_raw[:, 0, 0, 0, :], Wg[0, :, 0:P]).then_inc(wg0_in, 16)
            sp.dma_start(w_raw[:, 0, 0, 1, :], Wu[0, :, 0:P]).then_inc(wu0_in, 16)
            sp.dma_start(w_raw[:, 0, 1:NC, 0, :], Wg[0, :, rest].rearrange("p (c f) -> p c f", f=P)).then_inc(w0_in, 16)
            sp.dma_start(w_raw[:, 0, 1:NC, 1, :], Wu[0, :, rest].rearrange("p (c f) -> p c f", f=P)).then_inc(w0_in, 16)
            load_tile(X_ORDER[1])
            sp.dma_start(w_raw[:, 0, :, 2, :], Wd[0, :, :].rearrange("(c p) d -> p c d", p=P)).then_inc(wd0_in, 16)
            load_tile(X_ORDER[2])
            load_tile(X_ORDER[3])
            sp.dma_start(route_b[:, :, :], route.rearrange("(a b) e -> a b e", a=1).to_broadcast([P, B, E])).then_inc(c_in, 16)
            sp.dma_start(share_b[:, :], share.rearrange("(a b) -> a b", a=1).to_broadcast([P, B])).then_inc(c_in, 16)
            load_expert(1, Wg[1, :, :], Wu[1, :, :], Wd[1, :, :])
            sp.wait_ge(split_done, EARLY)
            with sp.Fori(1, E // 2) as pair:
                for slot in range(2):
                    sp.wait_ge(w_ready, 2 * NC * pair + NC * (slot - 1))
                    load_expert(slot, of_pair(Wg, pair, slot), of_pair(Wu, pair, slot), of_pair(Wd, pair, slot))
            with sp.Fori(0, B) as b:
                which = sp.value_load(step[bass.ds(b, 1)].rearrange("(a n) -> a n", a=1), min_val=1, max_val=K)
                sp.dma_start(T_nat[:, bass.ds(b, 1), :],
                             T[bass.ds(which - 1, 1), :, :].rearrange("a i j -> i a j")).then_inc(T_in, 16)
            sp.wait_ge(w_ready, NC * (E - 1))
            load_expert(0, Sg[:, :], Su[:, :], Sd[:, :])

            for i, (b, nb) in enumerate(parts):
                sp.wait_ge(res_done, i + 1)
                sp.dma_start(out[b:b + nb, :, :].rearrange("b s d -> s b d"), res[:, b:b + nb, :]).then_inc(stored, 16)
            sp.wait_ge(stored, 16 * len(parts))

        @block.gpsimd
        def _(pool):
            nc.gpsimd.memset(ident[:, :], 0.0).then_inc(ident_done, 1)
            pool.wait_ge(ident_done, 1)
            nc.gpsimd.affine_select(out=ident[:, :], in_=ident[:, :], compare_op=ALU.not_equal, fill=1.0, base=0,
                                    pattern=[[-1, P]], channel_multiplier=1).then_inc(ident_done, 1)

            def low_part(slot, c, m):
                return nc.gpsimd.tensor_tensor(w_lo[:, slot, c, m, :], w_raw[:, slot, c, m, :],
                                               w_hi[:, slot, c, m, :].bitcast(F32), ALU.subtract)

            def split_chunk(slot, c, count):
                nc.gpsimd.tensor_copy(w_hi[:, slot, c, :, :], w_raw[:, slot, c, :, :]).then_inc(w_rounded, 1)
                pool.wait_ge(w_rounded, count + 1)
                low_part(slot, c, slice(0, 3)).then_inc(w_ready, 1)

            pool.wait_ge(w0_rounded, 3)
            low_part(0, 1, slice(0, 2)).then_inc(w_ready, 1)
            pool.wait_ge(w0_rounded, 4)
            low_part(0, 2, slice(0, 2)).then_inc(w_ready, 1)
            low_part(0, 3, slice(0, 2)).then_inc(w_ready, 1)
            pool.wait_ge(w0_rounded, 5)
            low_part(0, slice(0, NC), 2).then_inc(w_ready, 1)

            for i, t in enumerate(X_ORDER[1:]):
                if t == 1:
                    pool.wait_ge(x_kept, 2)
                else:
                    pool.wait_ge(x_kept_late, i)
                nc.gpsimd.tensor_tensor(x_lo[:, t, :], acc[:, t, :], x_hi[:, t, :].bitcast(F32),
                                        ALU.subtract).then_inc(acc_done, 1)

            pool.wait_ge(c_in, 32)
            nc.gpsimd.tensor_scalar(rest_b[:, :], share_b[:, :], -1.0, 1.0, ALU.mult, ALU.add).then_inc(coef_step, 1)
            nc.gpsimd.tensor_copy(coef[:, E * B:(E + 1) * B], share_b[:, :]).then_inc(coef_step, 1)
            pool.wait_ge(coef_step, 2)
            nc.gpsimd.tensor_tensor(coef[:, 0:E * B].rearrange("p (e b) -> p b e", b=B), route_b[:, :, :],
                                    rest_b[:, :].unsqueeze(2).to_broadcast([P, B, E]), ALU.mult).then_inc(coef_step, 1)

            with pool.Fori(0, E, 2) as e:
                for par in range(2):
                    slot = (par + 1) % 2
                    for t in range(NT):
                        group = NT * (e + par) + t
                        if t == 0:
                            pool.wait_ge(w_in[slot], 24 * e + 48)
                        pool.wait_ge(acc_done, group + NT - 1)
                        pool.wait_ge(scaled_done, group + 1)
                        nc.gpsimd.tensor_tensor(acc[:, t, :], acc[:, t, :], scaled[:, t % 2, :], ALU.add).then_inc(acc_done, 1)
                        if t < 2:
                            for c in (2 * t, 2 * t + 1):
                                split_chunk(slot, c, NC * (e + par) + c)

            for t in range(NT):
                pool.wait_ge(g_read, turn_fill(t) + 1)
                turned = T_plus[:, t * BT:(t + 1) * BT, :]
                nc.gpsimd.tensor_tensor(turned, turned, ident[:, :].unsqueeze(1).to_broadcast([P, BT, P]),
                                        ALU.add).then_inc(T_done, 1)

        @block.scalar
        def _(act):
            def silu(n, k, turned):
                act.wait_ge(g_done, n + turned + 1)
                nc.scalar.activation(silu_g[:, k % 2, :], g_bank[(k + turned) % 2][:, :], ACT.Silu).then_inc(g_read, 1)

            def round_h(n, k):
                act.wait_ge(h_done, n + 1)
                nc.scalar.activation(h_hi[:, k % HR, :], u_bank[k % HR][:, :], ACT.Copy).then_inc(h_rounded, 1)

            def copy_y(i):
                b, nb = parts[i]
                act.wait_ge(y_turned, i + 1)
                nc.scalar.activation(y[:, b:b + nb, :], part_bank(i)[:, 0:nb * D].rearrange("p (b d) -> p b d", b=nb),
                                     ACT.Copy).then_inc(y_done, 1)

            def round_x(i):
                act.wait_ge(x_turned, i + 1)
                nc.scalar.activation(x_hi[:, X_ORDER[i], :], x_bank[X_ORDER[i]][:, :], ACT.Copy).then_inc(x_rounded, 1)

            def keep_x(i):
                nc.scalar.activation(acc[:, X_ORDER[i], :], x_bank[X_ORDER[i]][:, :], ACT.Copy).then_inc(x_kept_late, 1)

            def round_w0(c, m):
                nc.scalar.activation(w_hi[:, 0, c, m, :], w_raw[:, 0, c, m, :], ACT.Copy).then_inc(w0_rounded, 1)

            act.wait_ge(warm_done, 1)
            nc.scalar.activation(warm[:, :], warm[:, :], ACT.Silu)
            act.wait_ge(wg0_in, 16)
            round_w0(0, 0)
            act.wait_ge(wu0_in, 16)
            round_w0(0, 1)
            round_x(0)
            act.wait_ge(w0_in, 32)
            round_w0(1, slice(0, 2))
            round_w0(slice(2, NC), slice(0, 2))
            silu(0, 0, 0)
            act.wait_ge(wd0_in, 16)
            round_w0(slice(0, NC), 2)
            round_x(1)
            silu(1, 1, 0)
            round_h(0, 0)
            round_x(2)
            keep_x(2)
            silu(2, 2, 0)
            round_h(1, 1)
            round_x(3)
            keep_x(3)
            with act.Fori(0, N_ROUTED, U) as n0:
                for k in range(3, U + 3):
                    silu(n0 + k, k, 0)
                    round_h(n0 + k - 1, k - 1)
            for n in range(N_ROUTED + 3, N + 1):
                if n - FIRST_TURN in range(NT):
                    t = n - FIRST_TURN
                    act.wait_ge(g_done, turn_fill(t) + 1)
                    nc.scalar.activation(T_plus[:, t * BT:(t + 1) * BT, :],
                                         g_bank[turn_fill(t) % 2][:, :].rearrange("p (b i) -> p b i", b=BT),
                                         ACT.Copy).then_inc(g_read, 1)
                if n in COPY[:-1]:
                    copy_y(COPY.index(n))
                if n < N:
                    silu(n, n, turned_before(n))
                round_h(n - 1, n - 1)
            for i in range(NT - 2, len(parts)):
                copy_y(i)

        @block.vector
        def _(dve):
            def make_h(n, k):
                dve.wait_ge(g_read, n + turned_before(n) + 1)
                dve.wait_ge(u_done, n + 1)
                nc.vector.tensor_tensor(u_bank[k % HR][:, :], u_bank[k % HR][:, :], silu_g[:, k % 2, :],
                                        ALU.mult).then_inc(h_done, 1)

            def split_h(n, k):
                dve.wait_ge(h_rounded, n + 1)
                nc.vector.tensor_tensor(h_lo[:, k % HR, :], u_bank[k % HR][:, :], h_hi[:, k % HR, :].bitcast(F32),
                                        ALU.subtract).then_inc(split_done, 1)

            def scale_group(m0, t):
                dve.wait_ge(o_done, m0 + t + 1)
                dve.wait_ge(acc_done, m0 + t + NT - 2)
                nc.vector.tensor_tensor(scaled[:, t % 2, :].rearrange("p (b s) -> p b s", b=BT),
                                        o_bank[t % 2][:, :].rearrange("p (b s) -> p b s", b=BT),
                                        coef[:, bass.ds(m0 * BT + t * BT, BT)].unsqueeze(2).to_broadcast([P, BT, S]),
                                        ALU.mult).then_inc(scaled_done, 1)

            def add_shared(b):
                t, j = divmod(b, BT)
                s = slice(j * S, (j + 1) * S)
                nc.vector.scalar_tensor_tensor(out=yT[:, t, s], in0=o_bank[t % 2][:, s], scalar=coef[:, E * B + b:E * B + b + 1],
                                               in1=acc[:, t, s], op0=ALU.mult, op1=ALU.add).then_inc(yT_done, 1)

            def copy_result(i):
                b, nb = parts[i]
                dve.wait_ge(r_done, i + 1)
                nc.vector.tensor_copy(res[:, b:b + nb, :], part_bank(i)[:, 0:nb * D].rearrange("p (b d) -> p b d", b=nb))\
                    .then_inc(res_done, 1)

            def keep_x(t):
                nc.vector.tensor_copy(acc[:, t, :], x_bank[t][:, :]).then_inc(x_kept, 1)

            nc.vector.memset(warm[:, :], 0.0).then_inc(warm_done, 1)
            for m in range(2):
                dve.wait_ge(w0_rounded, m + 1)
                nc.vector.tensor_tensor(w_lo[:, 0, 0, m, :], w_raw[:, 0, 0, m, :], w_hi[:, 0, 0, m, :].bitcast(F32),
                                        ALU.subtract).then_inc(split_done, 1)
            dve.wait_ge(x_rounded, 1)
            nc.vector.tensor_tensor(x_lo[:, 0, :], x_bank[0][:, :], x_hi[:, 0, :].bitcast(F32),
                                    ALU.subtract).then_inc(split_done, 1)
            keep_x(0)
            make_h(0, 0)
            dve.wait_ge(x_rounded, 2)
            keep_x(1)
            make_h(1, 1)
            split_h(0, 0)
            make_h(2, 2)
            split_h(1, 1)
            with dve.Fori(0, E * NT, NT) as m0:
                for k in range(3, U + 3):
                    if k == NC + LAG:
                        dve.wait_ge(coef_step, 3)
                    if k in range(NC + LAG, U + 3, NC):
                        scale_group(m0, (k - NC - LAG) // NC)
                    make_h(m0 * NC + k, k)
                    split_h(m0 * NC + k - 1, k - 1)
            for n in range(N_ROUTED + 3, N + 1):
                for t in range(NT - 1):
                    if n == SCALE[t]:
                        dve.wait_ge(o_done, E * NT + t + 1)
                        dve.wait_ge(acc_done, NT - 1 + E * NT)
                        add_shared(t * BT)
                        add_shared(t * BT + 1)
                    if n == SCALE[t] + 1:
                        add_shared(t * BT + 2)
                        add_shared(t * BT + 3)
                    if n == STEP[t] and t < NT - 2:
                        copy_result(t)
                if n < N:
                    make_h(n, n)
                split_h(n - 1, n - 1)
            dve.wait_ge(o_done, E * NT + NT)
            for j in range(BT):
                add_shared((NT - 1) * BT + j)
            for i in range(NT - 2, len(parts)):
                copy_result(i)

        @block.tensor
        def _(pe):
            def product(bank, w, x_h, x_l, start, stop):
                nc.tensor.matmul(bank, w_hi[:, w[0], w[1], w[2], :], x_h, start=start, stop=False)
                nc.tensor.matmul(bank, w_hi[:, w[0], w[1], w[2], :], x_l, start=False, stop=False)
                return nc.tensor.matmul(bank, w_lo[:, w[0], w[1], w[2], :], x_h, start=False, stop=stop)

            def turn_x(i):
                t = X_ORDER[i]
                pe.wait_ge(x_in[t], 16)
                for j in range(BT):
                    last = nc.tensor.transpose(x_bank[t][:, j * S:(j + 1) * S], x_nat[:, t * BT + j, :], ident[:, :])
                last.then_inc(x_turned, 1)

            def project_g(n, k, turned):
                t, c = k % U // NC, k % NC
                pe.wait_ge(g_read, n + turned - 1)
                product(g_bank[(k + turned) % 2][:, :], (k // U % 2, c, 0), x_hi[:, t, :], x_lo[:, t, :],
                        True, True).then_inc(g_done, 1)

            def project_u(n, k):
                t, c = k % U // NC, k % NC
                if not (isinstance(n, int) and n < LAG):
                    pe.wait_ge(split_done, EARLY + n + 1 - HR)
                product(u_bank[k % HR][:, :], (k // U % 2, c, 1), x_hi[:, t, :], x_lo[:, t, :],
                        True, True).then_inc(u_done, 1)

            def project_down(n, k):
                t, c = k % U // NC, k % NC
                pe.wait_ge(split_done, EARLY + n + 1)
                last = product(o_bank[t % 2][:, :], (k // U % 2, c, 2), h_hi[:, k % HR, :], h_lo[:, k % HR, :],
                               c == 0, c == NC - 1)
                if c == NC - 1:
                    last.then_inc(o_done, 1)

            def turn_y(i):
                b, nb = parts[i]
                pe.wait_ge(yT_done, b + nb)
                for j in range(nb):
                    t, s = (b + j) // BT, ((b + j) % BT) * S
                    last = nc.tensor.transpose(part_bank(i)[:, j * D:(j + 1) * D], yT[:, t, s:s + S], ident[:, :])
                last.then_inc(y_turned, 1)

            def step_y(i):
                b, nb = parts[i]
                pe.wait_ge(y_done, i + 1)
                for j in range(nb):
                    last = nc.tensor.matmul(part_bank(i)[:, j * D:(j + 1) * D], T_plus[:, b + j, :], y[:, b + j, :],
                                            start=True, stop=True)
                last.then_inc(r_done, 1)

            def warm_up(n):
                for _ in range(n):
                    nc.tensor.matmul(o_bank[1][:, 0:P], ident[:, :], ident[:, :], start=True, stop=True)

            pe.wait_ge(ident_done, 2)
            warm_up(4)
            turn_x(0)
            warm_up(3)
            pe.wait_ge(x_rounded, 1)
            nc.tensor.matmul(g_bank[0][:, :], w_hi[:, 0, 0, 0, :], x_hi[:, 0, :], start=True, stop=False)
            pe.wait_ge(split_done, 1)
            nc.tensor.matmul(g_bank[0][:, :], w_lo[:, 0, 0, 0, :], x_hi[:, 0, :], start=False, stop=False)
            pe.wait_ge(split_done, EARLY)
            nc.tensor.matmul(g_bank[0][:, :], w_hi[:, 0, 0, 0, :], x_lo[:, 0, :], start=False, stop=True).then_inc(g_done, 1)
            project_u(0, 0)
            turn_x(1)
            pe.wait_ge(w_ready, 1)
            product(g_bank[1][:, :], (0, 1, 0), x_hi[:, 0, :], x_lo[:, 0, :], True, True).then_inc(g_done, 1)
            project_u(1, 1)
            pe.wait_ge(x_kept, 1)
            turn_x(2)
            turn_x(3)
            with pe.Fori(0, N_ROUTED // U, 2) as e:
                for k in range(LAG, 2 * U + LAG):
                    if k in (2, 3):
                        pe.wait_ge(w_ready, k)
                    if k % U == 0:
                        pe.wait_ge(w_ready, NC * (e + k // U + 1))
                    if k == NC:
                        pe.wait_ge(acc_done, 1)
                    if k == 2 * NC:
                        pe.wait_ge(acc_done, 3)
                    project_g(e * U + k, k, 0)
                    if k == 3:
                        pe.wait_ge(x_kept_late, 1)
                    project_u(e * U + k, k)
                    if k == LAG:
                        pe.wait_ge(w_ready, NC)
                    project_down(e * U + k - LAG, k - LAG)
            pe.wait_ge(T_in, 16 * B)
            for n in range(N_ROUTED + LAG, N):
                if n - FIRST_TURN in range(NT):
                    t = n - FIRST_TURN
                    pe.wait_ge(g_read, turn_fill(t) - 1)
                    for j in range(BT):
                        last = nc.tensor.transpose(g_bank[turn_fill(t) % 2][:, j * P:(j + 1) * P], T_nat[:, t * BT + j, :],
                                                   ident[:, :])
                    last.then_inc(g_done, 1)
                if n in STEP:
                    t = STEP.index(n)
                    if t == 0:
                        pe.wait_ge(T_done, NT)
                    step_y(t)
                project_g(n, n, turned_before(n))
                project_u(n, n)
                m = (n - LAG - N_ROUTED) // NC
                if (n - LAG) % NC == 0 and m >= 2:
                    pe.wait_ge(res_done, m - 1)
                for d in {N - 2: [], N - 1: [N - 4, N - 3]}.get(n, [n - LAG]):
                    project_down(d, d)
                if n in TURN:
                    turn_y(TURN.index(n))
            project_down(N - 2, N - 2)
            project_down(N - 1, N - 1)
            step_y(NT - 2)
            for j in range(BT):
                turn_y(NT - 1 + j)
            for j in range(BT):
                step_y(NT - 1 + j)


_INS = ["x", "fside_Bx8_0", "condB_sharedgateprob", "itok_B_1_98", "L0_cond_Wg", "L0_cond_Wu", "L0_cond_Wd",
        "L0_cond_Sg", "L0_cond_Su", "L0_cond_Sd", "L1_cond_T"]


def kernel(**inputs):
    import numpy as _np
    import concourse.bacc as _bacc
    from concourse import mybir as _mybir
    from concourse.bass_utils import run_bass_kernel_spmd as _run

    nc = _bacc.Bacc("TRN2", target_bir_lowering=False, num_devices=1)
    arrays, args = {}, []
    for name in _INS:
        a = _np.ascontiguousarray(inputs[name])
        arrays[f"in_{name}"] = a
        args.append(nc.dram_tensor(f"in_{name}", a.shape, _mybir.dt.from_np(a.dtype), kind="ExternalInput").ap())
    args.append(nc.dram_tensor("out_y", inputs["x"].shape, _mybir.dt.float32, kind="ExternalOutput").ap())
    moe_then_step_kernel(nc, *args)
    r = _run(nc, [arrays], core_ids=[0])
    return r.results[0]["out_y"]
```

```python
from contextlib import ExitStack

import concourse.bass as bass
from concourse import mybir

P = 128
F32 = mybir.dt.float32
F32R = mybir.dt.float32r
ALU = mybir.AluOpType
ACT = mybir.ActivationFunctionType


def moe_then_step_kernel(
    nc: bass.Bass,
    x: bass.AP,
    route: bass.AP,
    share: bass.AP,
    step: bass.AP,
    Wg: bass.AP,
    Wu: bass.AP,
    Wd: bass.AP,
    Sg: bass.AP,
    Su: bass.AP,
    Sd: bass.AP,
    T: bass.AP,
    out: bass.AP,
):
    B, S, D = x.shape
    E, _, F = Wg.shape
    K = T.shape[0]
    assert S == P and D == P
    NC = F // P
    BT = 4
    NT = B // BT
    W = BT * S
    U = NT * NC
    N_ROUTED = E * U
    N = N_ROUTED + U
    HR = 4
    LAG = 2
    PEEL_ACT = 6
    PEEL_DVE = 5
    EARLY = 3
    Q = 32
    assert NC == 4 and NT == 4 and E % 2 == 0

    with ExitStack() as ctx:
        def sb(name, shape, dt=F32):
            return ctx.enter_context(nc.sbuf_tensor(name, shape, dt))

        def sem(name):
            return ctx.enter_context(nc.semaphore(name))

        x_nat = sb("x_nat", [P, BT, D])
        x_blk = sb("x_blk", [P, B, S])
        zero = sb("zero", [P, P])
        silu_0 = sb("silu_0", [P, 1])
        x_hi = sb("x_hi", [P, NT, W], F32R)
        x_lo = sb("x_lo", [P, NT, W], F32R)
        w_raw = sb("w_raw", [P, 2, NC, 3, P])
        w_hi = sb("w_hi", [P, 2, NC, 3, P], F32R)
        w_lo = sb("w_lo", [P, 2, NC, 3, P], F32R)
        silu_g = sb("silu_g", [P, 2, W])
        h_hi = sb("h_hi", [P, HR, W], F32R)
        h_lo = sb("h_lo", [P, HR, W], F32R)
        scaled = sb("scaled", [P, 2, W])
        acc = sb("acc", [P, NT, W])
        yT = sb("yT", [P, NT, W])
        y = sb("y", [P, B, D])
        res = sb("res", [P, B, D])
        T_blk = sb("T_blk", [P, B, P])
        T_turn = sb("T_turn", [P, B, P])
        T_plus = sb("T_plus", [P, B, P])
        ident = sb("ident", [P, P])
        route_b = sb("route_b", [P, B, E])
        share_b = sb("share_b", [P, B])
        rest_b = sb("rest_b", [P, B])
        coef = sb("coef", [P, (E + 1) * B])

        g_bank = [ctx.enter_context(nc.psum_tensor(f"g_bank{i}", [P, W], F32)) for i in range(2)]
        u_bank = [ctx.enter_context(nc.psum_tensor(f"u_bank{i}", [P, W], F32)) for i in range(HR)]
        o_bank = [ctx.enter_context(nc.psum_tensor(f"o_bank{i}", [P, W], F32)) for i in range(2)]

        x_in = [sem(f"x_in{i}") for i in range(3)]
        wg0_in = sem("wg0_in")
        wu0_in = sem("wu0_in")
        w0_in = sem("w0_in")
        wd0_in = sem("wd0_in")
        w_in = [sem(f"w_in{s}") for s in range(2)]
        c_in = sem("c_in")
        T_in = [sem(f"T_in{q}") for q in range(P // Q)]
        zero_done = sem("zero_done")
        ident_done = sem("ident_done")
        coef_step = sem("coef_step")
        x0_turned = sem("x0_turned")
        x_turned = sem("x_turned")
        x_rounded = sem("x_rounded")
        w0_rounded = sem("w0_rounded")
        w_rounded = sem("w_rounded")
        w_ready = sem("w_ready")
        g_done = sem("g_done")
        g_read = sem("g_read")
        u_done = sem("u_done")
        h_done = sem("h_done")
        h_rounded = sem("h_rounded")
        split_done = sem("split_done")
        o_done = sem("o_done")
        scaled_done = sem("scaled_done")
        acc_done = sem("acc_done")
        T_turned = sem("T_turned")
        T_done = sem("T_done")
        yT_done = sem("yT_done")
        y_turned = sem("y_turned")
        y_done = sem("y_done")
        r_done = sem("r_done")
        res_done = sem("res_done")
        stored = sem("stored")

        parts = [(t * BT, BT) for t in range(NT - 1)] + [((NT - 1) * BT + b, 1) for b in range(BT)]
        last_part = len(parts) - 1
        parts_of = [[i for i, (b, _) in enumerate(parts) if b // BT == t] for t in range(NT)]

        def part_bank(i):
            b, nb = parts[i]
            return o_bank[(b // BT) % 2] if nb == BT else u_bank[b % BT]

        SCALE = [N_ROUTED + NC * t + NC + LAG for t in range(NT - 1)]
        TURN = [n + 1 for n in SCALE]
        COPY = [n + 2 for n in SCALE]
        STEP = [n + 3 for n in SCALE]
        TURN_T = [N_ROUTED + d for d in (5, 8, 9, 12)]

        block = ctx.enter_context(nc.Block())

        @block.sync
        def _(sp):
            def load_blocks(dst, m, sems):
                for q in range(P // Q):
                    sp.dma_start(dst[q * Q:(q + 1) * Q, :, :].rearrange("p n (r c) -> p (n r) c", c=Q),
                                 m[:, :, q * Q:(q + 1) * Q].rearrange("n (r p) c -> p (n r) c", p=Q)).then_inc(sems[q], 16)

            def load_expert(slot, gate, up, down):
                sp.dma_start(w_raw[:, slot, :, 0, :], gate.rearrange("p (c f) -> p c f", c=NC)).then_inc(w_in[slot], 16)
                sp.dma_start(w_raw[:, slot, :, 1, :], up.rearrange("p (c f) -> p c f", c=NC)).then_inc(w_in[slot], 16)
                sp.dma_start(w_raw[:, slot, :, 2, :], down.rearrange("(c p) d -> p c d", p=P)).then_inc(w_in[slot], 16)

            def of_pair(w, pair, slot):
                pairs = w.rearrange("(i s) p f -> i s p f", s=2)
                return pairs[bass.ds(pair, 1), slot, :, :].rearrange("i p f -> (i p) f")

            rest = slice(P, F)
            sp.dma_start(x_nat[:, :, :], x[0:BT, :, :].rearrange("b s d -> s b d")).then_inc(x_in[0], 16)
            sp.dma_start(w_raw[:, 0, 0, 0, :], Wg[0, :, 0:P]).then_inc(wg0_in, 16)
            sp.dma_start(w_raw[:, 0, 0, 1, :], Wu[0, :, 0:P]).then_inc(wu0_in, 16)
            sp.dma_start(w_raw[:, 0, 1:NC, 0, :], Wg[0, :, rest].rearrange("p (c f) -> p c f", f=P)).then_inc(w0_in, 16)
            sp.dma_start(w_raw[:, 0, 1:NC, 1, :], Wu[0, :, rest].rearrange("p (c f) -> p c f", f=P)).then_inc(w0_in, 16)
            load_blocks(x_blk[:, BT:2 * BT, :], x[BT:2 * BT, :, :], [x_in[1]] * 4)
            sp.dma_start(w_raw[:, 0, :, 2, :], Wd[0, :, :].rearrange("(c p) d -> p c d", p=P)).then_inc(wd0_in, 16)
            load_blocks(x_blk[:, 2 * BT:B, :], x[2 * BT:B, :, :], [x_in[2]] * 4)
            sp.dma_start(route_b[:, :, :], route.rearrange("(a b) e -> a b e", a=1).to_broadcast([P, B, E])).then_inc(c_in, 16)
            sp.dma_start(share_b[:, :], share.rearrange("(a b) -> a b", a=1).to_broadcast([P, B])).then_inc(c_in, 16)
            load_expert(1, Wg[1, :, :], Wu[1, :, :], Wd[1, :, :])
            sp.wait_ge(split_done, EARLY)
            with sp.Fori(1, E // 2) as pair:
                for slot in range(2):
                    sp.wait_ge(w_ready, 2 * NC * pair + NC * (slot - 1))
                    load_expert(slot, of_pair(Wg, pair, slot), of_pair(Wu, pair, slot), of_pair(Wd, pair, slot))
            with sp.Fori(0, B) as b:
                which = sp.value_load(step[bass.ds(b, 1)].rearrange("(a n) -> a n", a=1), min_val=1, max_val=K)
                load_blocks(T_blk[:, bass.ds(b, 1), :], T[bass.ds(which - 1, 1), :, :], T_in)
            sp.wait_ge(w_ready, NC * (E - 1))
            load_expert(0, Sg[:, :], Su[:, :], Sd[:, :])

            for first, last in [(i, i) for i in range(NT - 1)] + [(NT - 1, NT), (NT + 1, NT + 2)]:
                b0, b1 = parts[first][0], parts[last][0] + parts[last][1]
                sp.wait_ge(res_done, last + 1)
                sp.dma_start(out[b0:b1, :, :].rearrange("b s d -> s b d"), res[:, b0:b1, :]).then_inc(stored, 16)
            sp.wait_ge(stored, 16 * (NT + 1))

        @block.gpsimd
        def _(pool):
            nc.gpsimd.memset(ident[:, :], 0.0).then_inc(ident_done, 1)
            pool.wait_ge(ident_done, 1)
            nc.gpsimd.affine_select(out=ident[:, :], in_=ident[:, :], compare_op=ALU.not_equal, fill=1.0, base=0,
                                    pattern=[[-1, P]], channel_multiplier=1).then_inc(ident_done, 1)

            def low_part(slot, c, m):
                return nc.gpsimd.tensor_tensor(w_lo[:, slot, c, m, :], w_raw[:, slot, c, m, :],
                                               w_hi[:, slot, c, m, :].bitcast(F32), ALU.subtract)

            def split_chunk(slot, c, count):
                nc.gpsimd.tensor_copy(w_hi[:, slot, c, :, :], w_raw[:, slot, c, :, :]).then_inc(w_rounded, 1)
                pool.wait_ge(w_rounded, count + 1)
                low_part(slot, c, slice(0, 3)).then_inc(w_ready, 1)

            pool.wait_ge(w0_rounded, 3)
            low_part(0, 1, slice(0, 2)).then_inc(w_ready, 1)
            pool.wait_ge(w0_rounded, 4)
            low_part(0, 2, slice(0, 2)).then_inc(w_ready, 1)
            low_part(0, 3, slice(0, 2)).then_inc(w_ready, 1)
            pool.wait_ge(w0_rounded, 5)
            low_part(0, slice(0, NC), 2).then_inc(w_ready, 1)

            def split_x(t):
                pool.wait_ge(x_rounded, t + 1)
                nc.gpsimd.tensor_tensor(x_lo[:, t, :], acc[:, t, :], x_hi[:, t, :].bitcast(F32),
                                        ALU.subtract).then_inc(acc_done, 1)

            split_x(1)
            pool.wait_ge(c_in, 32)
            nc.gpsimd.tensor_scalar(rest_b[:, :], share_b[:, :], -1.0, 1.0, ALU.mult, ALU.add).then_inc(coef_step, 1)
            nc.gpsimd.tensor_copy(coef[:, E * B:(E + 1) * B], share_b[:, :]).then_inc(coef_step, 1)
            pool.wait_ge(coef_step, 2)
            nc.gpsimd.tensor_tensor(coef[:, 0:E * B].rearrange("p (e b) -> p b e", b=B), route_b[:, :, :],
                                    rest_b[:, :].unsqueeze(2).to_broadcast([P, B, E]), ALU.mult).then_inc(coef_step, 1)
            for t in range(2, NT):
                split_x(t)

            with pool.Fori(0, E, 2) as e:
                for par in range(2):
                    slot = (par + 1) % 2
                    for t in range(NT):
                        group = NT * (e + par) + t
                        if t == 0:
                            pool.wait_ge(w_in[slot], 24 * e + 48)
                        pool.wait_ge(acc_done, group + NT - 1)
                        pool.wait_ge(scaled_done, group + 1)
                        nc.gpsimd.tensor_tensor(acc[:, t, :], acc[:, t, :], scaled[:, t % 2, :], ALU.add).then_inc(acc_done, 1)
                        if t < 2:
                            for c in (2 * t, 2 * t + 1):
                                split_chunk(slot, c, NC * (e + par) + c)

            for t in range(NT):
                tile = slice(t * BT, (t + 1) * BT)
                pool.wait_ge(T_turned, t + 1)
                nc.gpsimd.tensor_tensor(T_plus[:, tile, :], T_turn[:, tile, :],
                                        ident[:, :].unsqueeze(1).to_broadcast([P, BT, P]), ALU.add).then_inc(T_done, 1)

        @block.scalar
        def _(act):
            def silu(n, k):
                act.wait_ge(g_done, n + 1)
                nc.scalar.activation(silu_g[:, k % 2, :], g_bank[k % 2][:, :], ACT.Silu).then_inc(g_read, 1)

            def round_h(n, k):
                act.wait_ge(h_done, n + 1)
                nc.scalar.activation(h_hi[:, k % HR, :], u_bank[k % HR][:, :], ACT.Copy).then_inc(h_rounded, 1)

            def copy_y(i):
                b, nb = parts[i]
                act.wait_ge(y_turned, i + 1)
                nc.scalar.activation(y[:, b:b + nb, :], part_bank(i)[:, 0:nb * D].rearrange("p (b d) -> p b d", b=nb),
                                     ACT.Copy).then_inc(y_done, 1)

            def round_x(t):
                act.wait_ge(x_turned, t)
                nc.scalar.activation(x_hi[:, t, :], acc[:, t, :], ACT.Copy).then_inc(x_rounded, 1)

            def round_w0(c, m):
                nc.scalar.activation(w_hi[:, 0, c, m, :], w_raw[:, 0, c, m, :], ACT.Copy).then_inc(w0_rounded, 1)

            act.wait_ge(zero_done, 1)
            nc.scalar.activation(silu_0[:, :], zero[:, 0:1], ACT.Silu)
            act.wait_ge(wg0_in, 16)
            round_w0(0, 0)
            act.wait_ge(wu0_in, 16)
            round_w0(0, 1)
            act.wait_ge(x0_turned, 1)
            nc.scalar.activation(x_hi[:, 0, :], o_bank[0][:, :], ACT.Copy).then_inc(x_rounded, 1)
            act.wait_ge(w0_in, 32)
            round_w0(1, slice(0, 2))
            round_w0(slice(2, NC), slice(0, 2))
            silu(0, 0)
            act.wait_ge(wd0_in, 16)
            round_w0(slice(0, NC), 2)
            silu(1, 1)
            round_h(0, 0)
            round_x(1)
            for n in range(2, PEEL_ACT):
                silu(n, n)
                round_h(n - 1, n - 1)
                if n >= PEEL_ACT - 2:
                    round_x(NT - PEEL_ACT + n)
            with act.Fori(0, N_ROUTED, U) as n0:
                for k in range(PEEL_ACT, U + PEEL_ACT):
                    silu(n0 + k, k)
                    round_h(n0 + k - 1, k - 1)
            for n in range(N_ROUTED + PEEL_ACT, N + 1):
                if n in COPY[:-1]:
                    copy_y(COPY.index(n))
                if n < N:
                    silu(n, n)
                round_h(n - 1, n - 1)
            for i in range(NT - 2, len(parts)):
                copy_y(i)

        @block.vector
        def _(dve):
            def make_h(n, k):
                dve.wait_ge(g_read, n + 1)
                dve.wait_ge(u_done, n + 1)
                nc.vector.tensor_tensor(u_bank[k % HR][:, :], u_bank[k % HR][:, :], silu_g[:, k % 2, :],
                                        ALU.mult).then_inc(h_done, 1)

            def split_h(n, k):
                dve.wait_ge(h_rounded, n + 1)
                nc.vector.tensor_tensor(h_lo[:, k % HR, :], u_bank[k % HR][:, :], h_hi[:, k % HR, :].bitcast(F32),
                                        ALU.subtract).then_inc(split_done, 1)

            def scale_group(m0, t):
                dve.wait_ge(o_done, m0 + t + 1)
                dve.wait_ge(acc_done, m0 + t + NT - 2)
                nc.vector.tensor_tensor(scaled[:, t % 2, :].rearrange("p (b s) -> p b s", b=BT),
                                        o_bank[t % 2][:, :].rearrange("p (b s) -> p b s", b=BT),
                                        coef[:, bass.ds(m0 * BT + t * BT, BT)].unsqueeze(2).to_broadcast([P, BT, S]),
                                        ALU.mult).then_inc(scaled_done, 1)

            def add_shared(b):
                t, j = divmod(b, BT)
                s = slice(j * S, (j + 1) * S)
                nc.vector.scalar_tensor_tensor(out=yT[:, t, s], in0=o_bank[t % 2][:, s], scalar=coef[:, E * B + b:E * B + b + 1],
                                               in1=acc[:, t, s], op0=ALU.mult, op1=ALU.add).then_inc(yT_done, 1)

            def copy_result(i):
                b, nb = parts[i]
                dve.wait_ge(r_done, i + 1)
                nc.vector.tensor_copy(res[:, b:b + nb, :], part_bank(i)[:, 0:nb * D].rearrange("p (b d) -> p b d", b=nb))\
                    .then_inc(res_done, 1)

            def turn_x(t):
                nc.vector.transpose(acc[:, t, :], x_blk[:, t * BT:(t + 1) * BT, :].rearrange("p b s -> p (b s)"))\
                    .then_inc(x_turned, 1)

            nc.vector.memset(zero[:, :], 0.0).then_inc(zero_done, 1)
            for m in range(2):
                dve.wait_ge(w0_rounded, m + 1)
                nc.vector.tensor_tensor(w_lo[:, 0, 0, m, :], w_raw[:, 0, 0, m, :], w_hi[:, 0, 0, m, :].bitcast(F32),
                                        ALU.subtract).then_inc(split_done, 1)
            dve.wait_ge(x_rounded, 1)
            nc.vector.tensor_tensor(x_lo[:, 0, :], o_bank[0][:, :], x_hi[:, 0, :].bitcast(F32),
                                    ALU.subtract).then_inc(split_done, 1)
            nc.vector.tensor_copy(acc[:, 0, :], o_bank[0][:, :])
            make_h(0, 0)
            dve.wait_ge(x_in[1], 64)
            turn_x(1)
            make_h(1, 1)
            split_h(0, 0)
            for n in range(2, PEEL_DVE):
                make_h(n, n)
                split_h(n - 1, n - 1)
                if n == PEEL_DVE - 2:
                    dve.wait_ge(x_in[2], 64)
                if n >= PEEL_DVE - 2:
                    turn_x(NT - PEEL_DVE + n)
            with dve.Fori(0, E * NT, NT) as m0:
                for k in range(PEEL_DVE, U + PEEL_DVE):
                    if k == NC + LAG:
                        dve.wait_ge(coef_step, 3)
                    if k in range(NC + LAG, U + PEEL_DVE, NC):
                        scale_group(m0, (k - NC - LAG) // NC)
                    make_h(m0 * NC + k, k)
                    split_h(m0 * NC + k - 1, k - 1)
            for n in range(N_ROUTED + PEEL_DVE, N + 1):
                for t in range(NT - 1):
                    if n == SCALE[t]:
                        dve.wait_ge(o_done, E * NT + t + 1)
                        dve.wait_ge(acc_done, NT - 1 + E * NT)
                        add_shared(t * BT)
                        add_shared(t * BT + 1)
                    if n == SCALE[t] + 1:
                        add_shared(t * BT + 2)
                        add_shared(t * BT + 3)
                    if n == STEP[t] and t < NT - 2:
                        copy_result(t)
                if n < N:
                    make_h(n, n)
                split_h(n - 1, n - 1)
                if n in TURN_T:
                    t = TURN_T.index(n)
                    if t == 0:
                        for q in range(P // Q):
                            dve.wait_ge(T_in[q], 16 * B)
                    tile = slice(t * BT, (t + 1) * BT)
                    nc.vector.transpose(T_turn[:, tile, :].rearrange("p b s -> p (b s)"),
                                        T_blk[:, tile, :].rearrange("p b s -> p (b s)")).then_inc(T_turned, 1)
            dve.wait_ge(o_done, E * NT + NT)
            for j in range(BT):
                add_shared((NT - 1) * BT + j)
            for i in range(NT - 2, len(parts)):
                copy_result(i)

        @block.tensor
        def _(pe):
            def product(bank, w, x_h, x_l, start, stop):
                nc.tensor.matmul(bank, w_hi[:, w[0], w[1], w[2], :], x_h, start=start, stop=False)
                nc.tensor.matmul(bank, w_hi[:, w[0], w[1], w[2], :], x_l, start=False, stop=False)
                return nc.tensor.matmul(bank, w_lo[:, w[0], w[1], w[2], :], x_h, start=False, stop=stop)

            def project_g(n, k):
                t, c = k % U // NC, k % NC
                pe.wait_ge(g_read, n - 1)
                product(g_bank[k % 2][:, :], (k // U % 2, c, 0), x_hi[:, t, :], x_lo[:, t, :],
                        True, True).then_inc(g_done, 1)

            def project_u(n, k):
                t, c = k % U // NC, k % NC
                if k >= LAG:
                    pe.wait_ge(split_done, EARLY + n + 1 - HR)
                product(u_bank[k % HR][:, :], (k // U % 2, c, 1), x_hi[:, t, :], x_lo[:, t, :],
                        True, True).then_inc(u_done, 1)

            def project_down(n, k):
                t, c, slot = k % U // NC, k % NC, k % HR
                w = (k // U % 2, c, 2)
                pe.wait_ge(h_rounded, n + 1)
                nc.tensor.matmul(o_bank[t % 2][:, :], w_hi[:, w[0], w[1], w[2], :], h_hi[:, slot, :], start=c == 0, stop=False)
                nc.tensor.matmul(o_bank[t % 2][:, :], w_lo[:, w[0], w[1], w[2], :], h_hi[:, slot, :], start=False, stop=False)
                pe.wait_ge(split_done, EARLY + n + 1)
                last = nc.tensor.matmul(o_bank[t % 2][:, :], w_hi[:, w[0], w[1], w[2], :], h_lo[:, slot, :],
                                        start=False, stop=c == NC - 1)
                if c == NC - 1:
                    last.then_inc(o_done, 1)

            def turn_y(i):
                b, nb = parts[i]
                pe.wait_ge(yT_done, b + nb)
                for j in range(nb):
                    t, s = (b + j) // BT, ((b + j) % BT) * S
                    last = nc.tensor.transpose(part_bank(i)[:, j * D:(j + 1) * D], yT[:, t, s:s + S], ident[:, :])
                last.then_inc(y_turned, 1)

            def step_y(i):
                b, nb = parts[i]
                pe.wait_ge(T_done, b // BT + 1)
                pe.wait_ge(y_done, i + 1)
                for j in range(nb):
                    last = nc.tensor.matmul(part_bank(i)[:, j * D:(j + 1) * D], T_plus[:, b + j, :], y[:, b + j, :],
                                            start=True, stop=True)
                last.then_inc(r_done, 1)

            def warm_up(n):
                for _ in range(n):
                    nc.tensor.matmul(o_bank[1][:, 0:P], zero[:, :], zero[:, :], start=True, stop=True)

            pe.wait_ge(zero_done, 1)
            warm_up(6)
            pe.wait_ge(ident_done, 2)
            pe.wait_ge(x_in[0], 16)
            for j in range(BT):
                last = nc.tensor.transpose(o_bank[0][:, j * S:(j + 1) * S], x_nat[:, j, :], ident[:, :])
            last.then_inc(x0_turned, 1)
            warm_up(2)
            pe.wait_ge(x_rounded, 1)
            nc.tensor.matmul(g_bank[0][:, :], w_hi[:, 0, 0, 0, :], x_hi[:, 0, :], start=True, stop=False)
            pe.wait_ge(split_done, 1)
            nc.tensor.matmul(g_bank[0][:, :], w_lo[:, 0, 0, 0, :], x_hi[:, 0, :], start=False, stop=False)
            pe.wait_ge(split_done, EARLY)
            nc.tensor.matmul(g_bank[0][:, :], w_hi[:, 0, 0, 0, :], x_lo[:, 0, :], start=False, stop=True).then_inc(g_done, 1)
            project_u(0, 0)
            pe.wait_ge(w_ready, 1)
            product(g_bank[1][:, :], (0, 1, 0), x_hi[:, 0, :], x_lo[:, 0, :], True, True).then_inc(g_done, 1)
            project_u(1, 1)
            with pe.Fori(0, N_ROUTED // U, 2) as e:
                for k in range(LAG, 2 * U + LAG):
                    if k in (2, 3):
                        pe.wait_ge(w_ready, k)
                    if k % U == 0:
                        pe.wait_ge(w_ready, NC * (e + k // U + 1))
                    if k in range(NC, U, NC):
                        pe.wait_ge(acc_done, k // NC)
                    project_g(e * U + k, k)
                    project_u(e * U + k, k)
                    if k == LAG:
                        pe.wait_ge(w_ready, NC)
                    project_down(e * U + k - LAG, k - LAG)
            for n in range(N_ROUTED + LAG, N):
                if n in STEP:
                    step_y(STEP.index(n))
                project_g(n, n)
                project_u(n, n)
                m = (n - LAG - N_ROUTED) // NC
                if (n - LAG) % NC == 0 and m >= 2:
                    pe.wait_ge(res_done, m - 1)
                for d in {N - 2: [], N - 1: [N - 4, N - 3]}.get(n, [n - LAG]):
                    project_down(d, d)
                if n in TURN:
                    turn_y(TURN.index(n))
            project_down(N - 2, N - 2)
            project_down(N - 1, N - 1)
            step_y(NT - 2)
            for j in range(BT):
                turn_y(NT - 1 + j)
            for j in range(BT):
                step_y(NT - 1 + j)


_INS = ["x", "fside_Bx8_0", "condB_sharedgateprob", "itok_B_1_98", "L0_cond_Wg", "L0_cond_Wu", "L0_cond_Wd",
        "L0_cond_Sg", "L0_cond_Su", "L0_cond_Sd", "L1_cond_T"]


def kernel(**inputs):
    import numpy as _np
    import concourse.bacc as _bacc
    from concourse import mybir as _mybir
    from concourse.bass_utils import run_bass_kernel_spmd as _run

    nc = _bacc.Bacc("TRN2", target_bir_lowering=False, num_devices=1)
    arrays, args = {}, []
    for name in _INS:
        a = _np.ascontiguousarray(inputs[name])
        arrays[f"in_{name}"] = a
        args.append(nc.dram_tensor(f"in_{name}", a.shape, _mybir.dt.from_np(a.dtype), kind="ExternalInput").ap())
    args.append(nc.dram_tensor("out_y", inputs["x"].shape, _mybir.dt.float32, kind="ExternalOutput").ap())
    moe_then_step_kernel(nc, *args)
    r = _run(nc, [arrays], core_ids=[0])
    return r.results[0]["out_y"]
```
